# Optimizing a Trainium2 kernel written in Bass

```python
import numpy as np
import jax
import jax.numpy as jnp

def _softmax(x, axis=-1):
    return jax.nn.softmax(x, axis=axis)

def _gelu(x):
    return jax.nn.gelu(x, approximate=True)

def _silu(x):
    return jax.nn.silu(x)

def _sigmoid(x):
    return jax.nn.sigmoid(x)

def _layernorm(x, axis=-1, eps=1e-05):
    m = jnp.mean(x, axis=axis, keepdims=True)
    v = jnp.var(x, axis=axis, keepdims=True)
    return (x - m) / jnp.sqrt(v + eps)

def _scatter_add(tgt, idx, src, axis=0):
    return tgt.at[idx].add(src)

def _segment_sum(src, seg, n):
    return jax.ops.segment_sum(src, seg, n)
kernel_name = 'mk_prb_d1_jaxref_r8_50e120'

def setup_inputs(seed: int=0):
    np.random.seed(seed)
    _w = jnp.asarray

    def _L0_attn_setup():
        import math
        import jax, jax.numpy as jnp
        import numpy as np
        N_HEADS = 16
        THETA = 10000.0

        def _rope_cos_sin(S, head_dim):
            half = head_dim // 2
            inv_freq = 1.0 / THETA ** (jnp.arange(half, dtype=jnp.float32) / half)
            t = jnp.arange(S, dtype=jnp.float32)
            freqs = t[:, None] * inv_freq[None, :]
            return (jnp.cos(freqs), jnp.sin(freqs))

        def _apply_rope(x, cos, sin):
            half = x.shape[-1] // 2
            x1, x2 = (x[..., :half], x[..., half:])
            c = cos[None, None, :, :]
            s = sin[None, None, :, :]
            return jnp.concatenate([x1 * c - x2 * s, x1 * s + x2 * c], axis=-1)
        key = jax.random.key(seed)
        k1, k2, k3 = jax.random.split(key, 3)
        B, S, D = (4, 256, 128)
        x = jax.random.normal(k1, (B, S, D), dtype=jnp.float32)
        w_qkv = jax.random.normal(k2, (3 * D, D), dtype=jnp.float32) * (1.0 / math.sqrt(D))
        w_out = jax.random.normal(k3, (D, D), dtype=jnp.float32) * (1.0 / math.sqrt(D))
        return {'x': x, 'w_qkv': w_qkv, 'w_out': w_out}
    _L0_attn_in = _L0_attn_setup()

    def _L0_ffn_setup():
        import jax, jax.numpy as jnp
        import numpy as np
        EMB = 128
        FF = 4 * EMB

        def _ternary(w):
            scale = jnp.maximum(jnp.mean(jnp.abs(w)), 1e-08)
            w_t = jnp.clip(jnp.round(w / scale), -1.0, 1.0)
            return w + jax.lax.stop_gradient(w_t - w)
        key = jax.random.key(seed)
        kx, k1, k2, kb1, kb2 = jax.random.split(key, 5)
        x = jax.random.normal(kx, (4, 256, EMB), dtype=jnp.float32)
        lim1 = 1.0 / np.sqrt(EMB)
        lim2 = 1.0 / np.sqrt(FF)
        W1 = jax.random.uniform(k1, (FF, EMB), jnp.float32, -lim1, lim1)
        b1 = jax.random.uniform(kb1, (FF,), jnp.float32, -lim1, lim1)
        W2 = jax.random.uniform(k2, (EMB, FF), jnp.float32, -lim2, lim2)
        b2 = jax.random.uniform(kb2, (EMB,), jnp.float32, -lim2, lim2)
        return {'x': x, 'W1': W1, 'b1': b1, 'W2': W2, 'b2': b2}
    _L0_ffn_in = _L0_ffn_setup()
    _d = {'L0_attn_x': _L0_attn_in['x'], 'L0_attn_w_qkv': _L0_attn_in['w_qkv'], 'L0_attn_w_out': _L0_attn_in['w_out'], 'L0_ffn_W1': _L0_ffn_in['W1'], 'L0_ffn_b1': _L0_ffn_in['b1'], 'L0_ffn_W2': _L0_ffn_in['W2'], 'L0_ffn_b2': _L0_ffn_in['b2']}
    _x0 = _d['L0_attn_x']
    _d['L0_attn_x'] = jax.random.normal(jax.random.fold_in(jax.random.key(seed), 1), (2, 1024, 128), dtype=_x0.dtype)
    del _x0
    return _d

def reference(L0_attn_x, L0_attn_w_qkv, L0_attn_w_out, L0_ffn_W1, L0_ffn_b1, L0_ffn_W2, L0_ffn_b2):

    def _L0_attn_ref(x, w_qkv, w_out):
        import math
        import jax, jax.numpy as jnp
        import numpy as np
        N_HEADS = 16
        THETA = 10000.0

        def _rope_cos_sin(S, head_dim):
            half = head_dim // 2
            inv_freq = 1.0 / THETA ** (jnp.arange(half, dtype=jnp.float32) / half)
            t = jnp.arange(S, dtype=jnp.float32)
            freqs = t[:, None] * inv_freq[None, :]
            return (jnp.cos(freqs), jnp.sin(freqs))

        def _apply_rope(x, cos, sin):
            half = x.shape[-1] // 2
            x1, x2 = (x[..., :half], x[..., half:])
            c = cos[None, None, :, :]
            s = sin[None, None, :, :]
            return jnp.concatenate([x1 * c - x2 * s, x1 * s + x2 * c], axis=-1)
        B, S, D = x.shape
        H = N_HEADS
        hd = D // H
        qkv = x @ w_qkv.T
        q, k, v = jnp.split(qkv, 3, axis=-1)

        def reshape(t):
            return t.reshape(B, S, H, hd).transpose(0, 2, 1, 3)
        q, k, v = (reshape(q), reshape(k), reshape(v))
        cos, sin = _rope_cos_sin(S, hd)
        q = _apply_rope(q.astype(jnp.float32), cos, sin).astype(x.dtype)
        k = _apply_rope(k.astype(jnp.float32), cos, sin).astype(x.dtype)
        scale = math.sqrt(hd)
        scores = jnp.einsum('bhsd,bhtd->bhst', q, k) / scale
        causal = jnp.tril(jnp.ones((S, S), dtype=bool))
        scores = jnp.where(causal[None, None], scores, -jnp.inf)
        attn = jax.nn.softmax(scores.astype(jnp.float32), axis=-1).astype(x.dtype)
        out = jnp.einsum('bhst,bhtd->bhsd', attn, v)
        out = out.transpose(0, 2, 1, 3).reshape(B, S, D)
        return out @ w_out.T

    def _L0_ffn_ref(x, W1, b1, W2, b2):
        import jax, jax.numpy as jnp
        import numpy as np
        EMB = 128
        FF = 4 * EMB

        def _ternary(w):
            scale = jnp.maximum(jnp.mean(jnp.abs(w)), 1e-08)
            w_t = jnp.clip(jnp.round(w / scale), -1.0, 1.0)
            return w + jax.lax.stop_gradient(w_t - w)
        h = jnp.einsum('bsd,fd->bsf', x, _ternary(W1)) + b1
        h = jax.nn.gelu(h, approximate=False)
        out = jnp.einsum('bsf,df->bsd', h, _ternary(W2)) + b2
        return out
    x = L0_attn_x
    xn = _layernorm(x, axis=-1)
    x = x + _L0_attn_ref(xn, L0_attn_w_qkv, L0_attn_w_out) + _L0_ffn_ref(xn, L0_ffn_W1, L0_ffn_b1, L0_ffn_W2, L0_ffn_b2)
    return x

_drawn_inputs = setup_inputs


def setup_inputs(seed=0):
    import zlib

    import numpy as np

    out = dict(_drawn_inputs(seed))
    spreads = {}
    factors = {'L0_attn_w_qkv': 8.0, 'L0_attn_w_out': 8.0, 'L0_ffn_b1': 8.0, 'L0_ffn_b2': 200.0}
    for name, (base, spread) in spreads.items():
        noise = np.random.default_rng([zlib.crc32(name.encode()), seed]).standard_normal(out[name].shape)
        drawn = base * np.exp(spread * noise) if base else spread * noise
        out[name] = jnp.asarray(drawn.astype(out[name].dtype))
    for name, factor in factors.items():
        out[name] = (out[name] * factor).astype(out[name].dtype)
    return out
```

```python
from contextlib import ExitStack

import concourse.bass as bass
from concourse import mybir

F32 = mybir.dt.float32
BF16 = mybir.dt.bfloat16
ALU = mybir.AluOpType
ACT = mybir.ActivationFunctionType
AX = mybir.AxisListType

P = 128
BANK = 512
BATCH, SEQ, D = 2, 1024, 128
HEADS, HD = 16, 8
FF = 512
TOK = BATCH * SEQ
TILES = TOK // P
CHUNKS = TOK // BANK
SEQ_TILES = SEQ // P
GH = 4
GROUPS = BATCH * HEADS // GH
GB = HEADS // GH
GW = GH * HD
PARTS = 3
PAIRS = PARTS * PARTS * HD
A_ROWS = 96
B_ROWS = A_ROWS + PARTS
STEPS = 12
A_RING, B_RING, P_RING, S_RING, SLOTS = 4, 2, 3, 4, 3
BIG = 3.0e38
SCALE = float(HD) ** -0.5
EPS = 1e-5


def row_unit(t):
    if t < 4:
        return 3 - t, 0, P * (4 - t), True
    if t % 2 == 0:
        return 4 + (t - 4) // 2, 0, BANK, False
    return 7 - (t - 5) // 2, BANK, P * (4 - (t - 5) // 2), True


def col_unit(t):
    if t < 4:
        return t, P * t, BANK - P * t, True
    if t % 2 == 0:
        return (t - 4) // 2, BANK, BANK, False
    d = (t - 5) // 2
    return 4 + d, BANK + P * d, BANK - P * d, True


def chunk_of(t):
    return 0 if t < 4 else 1


LAST_STEP = (3, 11)


def ring_units(first, last):
    units = []
    for t in range(STEPS):
        if t == 8:
            units.append((t, "before", "out0", None))
        if t == 5 and not last:
            units.append((t, "before", "max0", None))
        if t == 4 and not first:
            units.append((t, "before", "out1", None))
        if not last:
            units += [(t, "beside", "rows", h) for h in range(GH)]
        if t == 0:
            units.append((t, "after", "max1", None))
    return units


FIRST_TURN = ring_units(True, False)
TURN = ring_units(False, False)
LAST_TURN = ring_units(False, True)
PROLOGUE_UNITS = STEPS * GH + 1


def turn_units(i, r):
    return FIRST_TURN if is_first(i, r) else LAST_TURN if is_last(i, r) else TURN


def is_first(i, r):
    return isinstance(i, int) and 3 * i + r == 0


def is_last(i, r):
    return isinstance(i, int) and 3 * i + r == GROUPS - 1


def ring_base(i, r):
    if is_first(i, r):
        return PROLOGUE_UNITS
    return PROLOGUE_UNITS + len(FIRST_TURN) - len(TURN) + len(TURN) * r + 3 * len(TURN) * i


def ring_const(i, r):
    if is_first(i, r):
        return PROLOGUE_UNITS % A_RING
    return (PROLOGUE_UNITS + len(FIRST_TURN)) % A_RING


assert len(TURN) % A_RING == 0


def ring_at(i, r, kind):
    return ring_base(i, r) + next(n for n, u in enumerate(turn_units(i, r)) if u[2] == kind)


def max_at(i, r, half):
    if half:
        return ring_at(i, r, "max1") + (not isinstance(i, int) and r == 0)
    if is_first(i, r):
        return GH * 5
    return ring_at(i, r - 1, "max0")


FFN_AFTER = [2, 2, 1, 2, 2, 1, 2, 2, 1, 0, 0, 1]


def start_units():
    early = []
    for b in range(BATCH):
        cs = (2 * b, 2 * b + 1)
        early += [("xT", c) for c in cs]
        for c in cs:
            early += [("proj", c, z) for z in range(4)]
        early += [("v", c) for c in cs]
    early.append(("scale",))
    up = [[("up", c, f) for f in range(FF // P)] + [("down", c)] for c in range(CHUNKS)]
    return early, up


EARLY, FFN = start_units()
FFN_ORDER = FFN[0][:4] + FFN[1][:4] + FFN[0][4:] + FFN[2][:4] + FFN[1][4:] + FFN[3][:4] + FFN[2][4:] + FFN[3][4:]
START = EARLY + FFN_ORDER
EMPTIED_BY = {"xT": "act", "proj": "dve", "v": "act", "scale": "dve", "up": "act", "down": "dve"}


def emptied(n):
    who = EMPTIED_BY[START[n][0]]
    return who, sum(EMPTIED_BY[u[0]] == who for u in START[:n + 1])


def build(nc, x, wqkv, wswap, wo, w1, b1, w2, b2, cos, sin, const_rows, out):
    q_scratch, k_scratch = (nc.dram_tensor(name, (PARTS, HD, 2, GROUPS * GH, BANK), BF16, kind="Internal").ap()
                            for name in ("q_parts", "k_parts"))
    scratch = (q_scratch, k_scratch)

    with ExitStack() as ctx:
        def sb(name, shape, dt=F32):
            return ctx.enter_context(nc.sbuf_tensor(name, shape, dt))

        def sem(name):
            return ctx.enter_context(nc.semaphore(name))

        banks = ctx.enter_context(nc.psum_tensor("banks", [P, 8, BANK], F32))
        A_BANK, B_BANK, O_BANK, S_BANK = 0, 4, 6, 4

        x_sb = sb("x_sb", [P, TILES, D])
        xn = sb("xn", [P, TILES, D])
        xnT = sb("xnT", [P, TOK])
        stats = sb("stats", [P, TILES, 6])
        mean_var = sb("mean_var", [P, TILES, 2])
        std = sb("std", [P, TILES])
        rstd = sb("rstd", [P, TILES])
        eps = sb("eps", [P, 1])
        wqkv_sb = sb("wqkv_sb", [P, 3 * D])
        wswap_sb = sb("wswap_sb", [P, 2 * D])
        wo_sb = sb("wo_sb", [P, D])
        w1_sb = sb("w1_sb", [P, FF])
        w1_t = sb("w1_t", [P, FF])
        w2_sb = sb("w2_sb", [P, FF // P, D])
        w2_t = sb("w2_t", [P, FF // P, D])
        b1_sb = sb("b1_sb", [P, FF // P])
        b2_sb = sb("b2_sb", [P, D])
        w_sums = sb("w_sums", [P, 2])
        limit = sb("limit", [P, 2])
        neg_limit = sb("neg_limit", [P, 2])
        below = sb("below", [P, FF])
        cos_sb = sb("cos_sb", [P, SEQ])
        sin_sb = sb("sin_sb", [P, SEQ])
        ident = sb("ident", [P, P])
        ident_b = sb("ident_b", [P, P], BF16)
        ones = sb("ones", [P, P])
        causal = sb("causal", [P, BANK])
        future = sb("future", [P, P], BF16)
        rot_a = sb("rot_a", [P, 2, BANK])
        rot_b = sb("rot_b", [P, 2, BANK])
        rotated = sb("rotated", [P, 2, BANK])
        rest = sb("rest", [P, 2, BANK])
        parts = sb("parts", [P, 2, PARTS, BANK], BF16)
        hT = sb("hT", [P, 2, FF // P, BANK])
        base = sb("base", [P, TILES, D])
        v_all = sb("v_all", [P, GROUPS, SEQ_TILES, GW])
        q_op = [sb(f"q_op{s}", [P, 2, GH, BANK], BF16) for s in range(SLOTS)]
        k_op = [sb(f"k_op{s}", [P, 2, GH, BANK], BF16) for s in range(SLOTS)]
        v_op = [sb(f"v_op{s}", [P, SEQ_TILES, GH, 32]) for s in range(SLOTS)]
        junk = sb("junk", [P, A_RING, BANK], BF16)
        maxima = sb("maxima", [P, 3, GH, 4])
        max_rest = sb("max_rest", [P, 2, GH * 4])
        max_parts = sb("max_parts", [P, 2, PARTS, GH * 4], BF16)
        max_rows = sb("max_rows", [PARTS * GH * 4, 2, P], BF16)
        probs = sb("probs", [P, P_RING, GH, BANK])
        o_T = sb("o_T", [P, 2, BANK])
        recip = sb("recip", [P, 2, 4, GH])
        attn = sb("attn", [P, SEQ_TILES, GROUPS, GW])
        attnT = xnT[:, :].rearrange("p (u n) -> p u n", u=4)
        result = x_sb[:, :, :].rearrange("p (u t) d -> p u (t d)", u=4)

        x_in = [sem(f"x_in{c}") for c in range(CHUNKS)]
        wqk_in, wffn_in, b_in, table_in = sem("wqk_in"), sem("wffn_in"), sem("b_in"), sem("table_in")
        pool_const = sem("pool_const")
        rows_in = sem("rows_in")
        dve_step = sem("dve_step")
        apart = sem("apart")
        pool_step = sem("pool_step")
        eps_set, var_ready, std_ready, xn_ready = sem("eps_set"), sem("var_ready"), sem("std_ready"), sem("xn_ready")
        xnT_ready = sem("xnT_ready")
        wsum_ready, wt_ready = sem("wsum_ready"), sem("wt_ready")
        s_full, s_act, s_dve = sem("s_full"), sem("s_act"), sem("s_dve")
        rot_ready, part0, rest_ready, part1, part2 = (
            sem("rot_ready"), sem("part0"), sem("rest_ready"), sem("part1"), sem("part2"))
        parts_out = [sem("parts_out0"), sem("parts_out1")]
        xb_ready = sem("xb_ready")
        op_in = [sem(f"op_in{s}") for s in range(SLOTS)]
        v_ready = sem("v_ready")
        a_full, a_free = sem("a_full"), sem("a_free")
        max_split = sem("max_split")
        max_in = [sem("max_in0"), sem("max_in1")]
        b_full, exp_done = sem("b_full"), sem("exp_done")
        pv_done = sem("pv_done")
        o_out = sem("o_out")
        recip_ready = sem("recip_ready")
        t_full, t_copied, y_full, y_added = sem("t_full"), sem("t_copied"), sem("y_full"), sem("y_added")
        out_done = sem("out_done")

        block = ctx.enter_context(nc.Block())
        x_tiles = x.rearrange("b (t p) d -> p (b t) d", p=P)
        out_tiles = out.rearrange("b (t p) d -> p (b t) d", p=P)

        def store_parts(eng, y):
            c, z = y // 2, y % 2
            eng.wait_ge(part2, y + 1)
            b, half = c // 2, c % 2
            for a in range(PARTS):
                eng.dma_start(scratch[z][a, :, half, HEADS * b:HEADS * (b + 1), :].rearrange("d h n -> h d n"),
                              parts[:, y % 2, a, :]).then_inc(parts_out[y % 2], 16)

        def load_ops(eng, i, r):
            g, s = 3 * i + r, r % SLOTS

            def load(op, source, row, part, parts_n):
                src = source[part:part + parts_n, :, :, bass.ts(g, GH), :].rearrange("a d c h n -> (a d) c (h n)")
                dst = op[HD * row:HD * (row + parts_n), :, :, :].rearrange("p c h n -> p c (h n)")
                eng.dma_start(dst, src).then_inc(op_in[s], 16)

            for u in range(PARTS):
                load(k_op[s], k_scratch, PARTS * u, 0, PARTS)
                load(q_op[s], q_scratch, PARTS * u, u, PARTS - u)
                if u:
                    load(q_op[s], q_scratch, PARTS * u + PARTS - u, 0, u)

        OP_DMAS = 16 * (3 * PARTS - 1)

        def load_max(eng, i, r, half):
            g, s = 3 * i + r, r % SLOTS
            eng.wait_ge(a_free, max_at(i, r, half) + 1)
            for a in range(PARTS):
                eng.dma_start(q_op[s][A_ROWS + a:A_ROWS + a + 1, half, :, :].rearrange("o h (i n) -> o (h i) n", n=P),
                              max_rows[16 * a:16 * a + 16, half, :]).then_inc(max_in[half], 16)

        @block.sync
        def _(sp):
            for c in range(CHUNKS):
                sp.dma_start(x_sb[:, 4 * c:4 * c + 4, :], x_tiles[:, 4 * c:4 * c + 4, :]).then_inc(x_in[c], 16)
            sp.dma_start(cos_sb[:, :], cos).then_inc(table_in, 16)
            sp.dma_start(sin_sb[:, :], sin).then_inc(table_in, 16)
            for s in range(SLOTS):
                sp.dma_start(q_op[s][PAIRS:A_ROWS, :, :, :].rearrange("p c h n -> p (c h n)"),
                             const_rows[0:A_ROWS - PAIRS, :]).then_inc(rows_in, 16)
                sp.dma_start(k_op[s][PAIRS:B_ROWS, :, :, :].rearrange("p c h n -> p (c h n)"),
                             const_rows).then_inc(rows_in, 16)
            for b in range(BATCH):
                for y in range(4 * b, 4 * b + 4):
                    store_parts(sp, y)
                sp.wait_ge(parts_out[0], 16 * PARTS * 2 * (b + 1))
                sp.wait_ge(parts_out[1], 16 * PARTS * 2 * (b + 1))
                if b == 0:
                    load_ops(sp, 0, 0)
                    load_ops(sp, 0, 1)
            load_max(sp, 0, 0, 0)

            def turn(i, r):
                g = 3 * i + r
                if not (isinstance(i, int) and g + 2 >= GROUPS):
                    sp.wait_ge(b_full, STEPS * GH * g + 1)
                    load_ops(sp, i, r + 2)
                load_max(sp, i, r, 1)
                if not is_last(i, r):
                    load_max(sp, i, r + 1, 0)

            with sp.Fori(0, (GROUPS - 2) // 3) as i:
                for r in range(3):
                    turn(i, r)
            turn(0, GROUPS - 2)
            turn(0, GROUPS - 1)
            for u in range(4):
                sp.wait_ge(y_added, u + 1)
                sp.dma_start(out_tiles[:, 4 * u:4 * u + 4, :],
                             result[:, u, :].rearrange("p (t d) -> p t d", d=D)).then_inc(out_done, 16)
            sp.wait_ge(out_done, 64)

        @block.gpsimd
        def _(pool):
            pool.memset(ident[:, :], 0.0).then_inc(pool_step, 1)
            pool.memset(causal[:, :], 0.0).then_inc(pool_step, 1)
            pool.memset(future[:, :], 0.0).then_inc(pool_step, 1)
            pool.memset(ones[:, :], 1.0).then_inc(pool_const, 1)
            pool.wait_ge(pool_step, 3)
            pool.affine_select(out=ident[:, :], in_=ident[:, :], compare_op=ALU.not_equal, fill=1.0, base=0,
                               pattern=[[-1, P]], channel_multiplier=1).then_inc(pool_const, 1)
            pool.affine_select(out=future[:, :], in_=future[:, :], compare_op=ALU.is_ge, fill=-BIG, base=0,
                               pattern=[[1, P]], channel_multiplier=-1).then_inc(pool_const, 1)
            pool.affine_select(out=causal[:, BANK - P:BANK], in_=causal[:, BANK - P:BANK], compare_op=ALU.is_ge,
                               fill=-BIG, base=0, pattern=[[-1, P]], channel_multiplier=1).then_inc(pool_const, 1)
            pool.wait_ge(pool_const, 4)
            pool.tensor_copy(ident_b[:, :], ident[:, :]).then_inc(pool_const, 1)
            for s in range(SLOTS):
                pool.memset(v_op[s][:, :, :, HD:32], 0.0).then_inc(pool_const, 1)
            pool.wait_ge(pool_const, 8)
            for s in range(SLOTS):
                pool.memset(v_op[s][:, :, :, HD:HD + 1], 1.0).then_inc(pool_const, 1)

            def split(y):
                pool.wait_ge(part0, y + 1)
                pool.tensor_tensor(rest[:, y % 2, :], rotated[:, y % 2, :], parts[:, y % 2, 0, :],
                                   ALU.subtract).then_inc(rest_ready, 1)
                pool.wait_ge(part1, y + 1)
                pool.tensor_tensor(parts[:, y % 2, 2, :], rest[:, y % 2, :], parts[:, y % 2, 1, :],
                                   ALU.subtract).then_inc(part2, 1)

            for y in range(4):
                split(y)
            for c in range(CHUNKS):
                pool.wait_ge(x_in[c], 16)
            pool.wait_ge(b_in, 32)
            pool.tensor_tensor(base[:, :, :], x_sb[:, :, :], b2_sb[:, :].unsqueeze(1).to_broadcast([P, TILES, D]),
                               ALU.add).then_inc(xb_ready, 1)
            for y in range(4, 8):
                split(y)

            def fill_v(i, r):
                g, s = 3 * i + r, r % SLOTS
                pool.tensor_copy(v_op[s][:, :, :, 0:HD],
                                 v_all[:, g, :, :].rearrange("p t (h d) -> p t h d", d=HD)).then_inc(v_ready, 1)

            def turn(i, r):
                if not is_first(i, r):
                    pool.wait_ge(pv_done, STEPS * (3 * i + r - 1))
                    pool.sem_inc(apart, 1)
                fill_v(i, r + 1)

            pool.wait_ge(s_act, emptied(START.index(("v", CHUNKS - 1)))[1])
            fill_v(0, 0)
            turn(0, 0)
            with pool.Fori(0, (GROUPS - 2) // 3) as i:
                for r in (1, 2, 3):
                    turn(i, r)

        @block.vector
        def _(dve):
            own = [0]

            def mark(instruction):
                own[0] += 1
                instruction.then_inc(dve_step, 1)
                return own[0]

            dve.memset(eps[:, :], EPS).then_inc(eps_set, 1)

            def normalise(b):
                for c in (2 * b, 2 * b + 1):
                    dve.wait_ge(x_in[c], 16)
                    for t in range(4 * c, 4 * c + 4):
                        last = mark(dve.bn_stats(stats[:, t, :], x_sb[:, t, :]))
                dve.wait_ge(dve_step, last)
                for t in range(SEQ_TILES * b, SEQ_TILES * (b + 1)):
                    dve.bn_aggr(mean_var[:, t, :], stats[:, t, :]).then_inc(var_ready, 1)
                dve.wait_ge(var_ready, SEQ_TILES * (b + 1))
                tiles = slice(SEQ_TILES * b, SEQ_TILES * (b + 1))
                dve.wait_ge(std_ready, b + 1)
                last = mark(dve.reciprocal(rstd[:, tiles], std[:, tiles]))
                dve.wait_ge(dve_step, last)
                for t in range(SEQ_TILES * b, SEQ_TILES * (b + 1)):
                    dve.tensor_scalar(xn[:, t, :], x_sb[:, t, :], mean_var[:, t, 0:1], rstd[:, t:t + 1],
                                      ALU.subtract, ALU.mult).then_inc(xn_ready, 1)

            def rotate(c):
                at = (c % 2) * BANK
                for z in range(2):
                    y = 2 * c + z
                    if y >= 2:
                        dve.wait_ge(part1, y - 1)
                        dve.wait_ge(part2, y - 1)
                    for half, (buf, table) in enumerate(((rot_a, cos_sb), (rot_b, sin_sb))):
                        n = START.index(("proj", c, 2 * z + half))
                        dve.wait_ge(s_full, n + 1)
                        dve.tensor_tensor(buf[:, y % 2, :], banks[:, S_BANK + n % S_RING, :],
                                          table[:, at:at + BANK], ALU.mult).then_inc(s_dve, 1)
                    dve.wait_ge(s_dve, emptied(n)[1])
                    dve.tensor_tensor(rotated[:, y % 2, :], rot_a[:, y % 2, :], rot_b[:, y % 2, :],
                                      ALU.add).then_inc(rot_ready, 1)

            normalise(0)
            dve.wait_ge(table_in, 32)
            rotate(0)
            rotate(1)
            normalise(1)

            dve.wait_ge(wffn_in, 48)
            dve.tensor_reduce(w_sums[:, 0:1], w1_sb[:, :], AX.X, ALU.add,
                              apply_absolute_value=True).then_inc(wsum_ready, 1)
            dve.tensor_reduce(w_sums[:, 1:2], w2_sb[:, :, :], AX.XY, ALU.add,
                              apply_absolute_value=True).then_inc(wsum_ready, 1)
            rotate(2)
            rotate(3)
            n = START.index(("scale",))
            dve.wait_ge(s_full, n + 1)
            dve.tensor_scalar(limit[:, :], banks[:, S_BANK + n % S_RING, 0:2], 1.0 / (FF * D), 1e-8,
                              ALU.mult, ALU.max).then_inc(s_dve, 1)
            dve.wait_ge(s_dve, emptied(n)[1])
            mark(dve.tensor_scalar(neg_limit[:, :], limit[:, :], -0.5, None, ALU.mult))
            dve.wait_ge(dve_step, own[0])
            mark(dve.tensor_scalar(limit[:, :], neg_limit[:, :], -1.0, None, ALU.mult))
            dve.wait_ge(dve_step, own[0])
            for k, (w, w_t) in enumerate(((w1_sb[:, :], w1_t[:, :]),
                                          (w2_sb[:, :, :].rearrange("p f d -> p (f d)"),
                                           w2_t[:, :, :].rearrange("p f d -> p (f d)")))):
                if k == 1:
                    dve.wait_ge(wt_ready, 1)
                mark(dve.tensor_scalar(below[:, :], w, neg_limit[:, k:k + 1], None, ALU.is_lt))
                dve.wait_ge(dve_step, own[0])
                dve.scalar_tensor_tensor(out=w_t, in0=w, scalar=limit[:, k:k + 1], in1=below[:, :],
                                         op0=ALU.is_gt, op1=ALU.subtract).then_inc(wt_ready, 1)

            def add_ffn(c):
                n = START.index(("down", c))
                if c == 0:
                    dve.wait_ge(xb_ready, 1)
                dve.wait_ge(s_full, n + 1)
                tile4 = base[:, 4 * c:4 * c + 4, :].rearrange("p t d -> p (t d)")
                dve.tensor_tensor(tile4, banks[:, S_BANK + n % S_RING, :], tile4, ALU.add).then_inc(s_dve, 1)

            def rows(slot, t, h):
                i, _, n, diagonal = row_unit(t)
                scores = banks[:, A_BANK + slot, 0:n]
                which = 0 if t < 4 else 1 + t % 2
                into = maxima[:, which, h, i % 4:i % 4 + 1]
                if diagonal:
                    dve.tensor_tensor_reduce(junk[:, slot, 0:n], scores, causal[:, BANK - n:BANK], 1.0, -BIG,
                                             ALU.add, ALU.max, into).then_inc(a_free, 1)
                else:
                    dve.tensor_reduce(into, scores, AX.X, ALU.max).then_inc(a_free, 1)

            def split_max(i, r, half, emptied_units):
                done = 9 * (3 * i + r) + 4 * half
                first, upper, lower = (maxima[:, w, :, :].rearrange("p h i -> p (h i)") for w in range(3))
                whole = upper if half else first
                part = [max_parts[:, half, a, :] for a in range(PARTS)]
                dve.wait_ge(a_free, emptied_units)
                if half:
                    dve.tensor_tensor(upper, upper, lower, ALU.max).then_inc(max_split, 1)
                    done = done + 1
                    dve.wait_ge(max_split, done)
                dve.tensor_copy(part[0], whole).then_inc(max_split, 1)
                dve.wait_ge(max_split, done + 1)
                dve.tensor_tensor(max_rest[:, 0, :], whole, part[0], ALU.subtract).then_inc(max_split, 1)
                dve.wait_ge(max_split, done + 2)
                dve.tensor_copy(part[1], max_rest[:, 0, :]).then_inc(max_split, 1)
                dve.wait_ge(max_split, done + 3)
                dve.tensor_tensor(part[2], max_rest[:, 0, :], part[1], ALU.subtract).then_inc(max_split, 1)

            def copy_max(slot, i, r, half):
                g = 3 * i + r
                if not is_first(i, r):
                    dve.wait_ge(max_in[half], 16 * PARTS * g)
                rows_T = banks[0:PARTS * GH * 4, A_BANK + slot, :].bitcast(BF16)[:, 0:P]
                dve.tensor_copy(max_rows[:, half, :], rows_T).then_inc(a_free, 1)

            def divide(slot, i, r, half):
                g = 3 * i + r
                turned = banks[:, A_BANK + slot, :].rearrange("p (t h w) -> p t h w", t=4, h=GH)
                dve.reciprocal(recip[:, half, :, :], turned[:, :, :, HD]).then_inc(recip_ready, 1)
                dve.wait_ge(recip_ready, 2 * g + half + 1)
                into = attn[:, 4 * half:4 * half + 4, g, :].rearrange("p t (h d) -> p t h d", d=HD)
                dve.tensor_tensor(into, turned[:, :, :, 0:HD],
                                  recip[:, half, :, :].unsqueeze(3).to_broadcast([P, 4, GH, HD]),
                                  ALU.mult).then_inc(a_free, 1)

            def turn(i, r):
                units = turn_units(i, r)
                first = ring_base(i, r)
                for u, (t, _, kind, h) in enumerate(units):
                    slot = (ring_const(i, r) + u) % A_RING
                    dve.wait_ge(a_full, first + u + 1)
                    if kind == "rows" and row_unit(t)[3]:
                        dve.sem_inc(apart, 1)
                    if kind == "rows":
                        rows(slot, t, h)
                    elif kind == "max1":
                        copy_max(slot, i, r, 1)
                    elif kind == "max0":
                        copy_max(slot, i, r + 1, 0)
                    elif kind == "out1":
                        divide(slot, i, r - 1, 1)
                    else:
                        divide(slot, i, r, 0)
                    if kind == "rows" and h == GH - 1 and t in LAST_STEP:
                        split_max(i, r + 1, LAST_STEP.index(t), first + u + 1)

            dve.wait_ge(pool_const, 4)
            ffn = list(FFN_ORDER[4:])
            for t in range(STEPS):
                if t == 5:
                    dve.wait_ge(a_full, GH * 5 + 1)
                    copy_max(GH * 5 % A_RING, 0, 0, 0)
                for h in range(GH):
                    u = GH * t + h + (t >= 5)
                    dve.wait_ge(a_full, u + 1)
                    rows(u % A_RING, t, h)
                if t in LAST_STEP:
                    split_max(0, 0, LAST_STEP.index(t), GH * (t + 1) + (t >= 5))
                for _ in range(FFN_AFTER[t]):
                    unit = ffn.pop(0)
                    if unit[0] == "down":
                        add_ffn(unit[1])
            turn(0, 0)
            with dve.Fori(0, (GROUPS - 2) // 3) as i:
                for r in (1, 2, 3):
                    turn(i, r)
            turn(0, GROUPS - 1)
            end = ring_base(0, GROUPS - 1) + len(LAST_TURN)
            dve.wait_ge(a_full, end + 1)
            divide(end % A_RING, 0, GROUPS - 1, 1)
            for u in range(4):
                dve.wait_ge(y_full, u + 1)
                dve.tensor_tensor(result[:, u, :], banks[:, B_BANK + u, :],
                                  base[:, 4 * u:4 * u + 4, :].rearrange("p t d -> p (t d)"),
                                  ALU.add).then_inc(y_added, 1)

        @block.scalar
        def _(act):
            act.dma_start(wqkv_sb[:, :], wqkv).then_inc(wqk_in, 16)
            act.dma_start(wswap_sb[:, :], wswap).then_inc(wqk_in, 16)
            act.dma_start(w1_sb[:, :], w1).then_inc(wffn_in, 16)
            act.dma_start(w2_sb[:, :, :], w2).then_inc(wffn_in, 16)
            act.dma_start(wo_sb[:, :], wo).then_inc(wffn_in, 16)
            act.dma_start(b1_sb[:, :], b1).then_inc(b_in, 16)
            act.dma_start(b2_sb[:, :], b2.to_broadcast([P, D])).then_inc(b_in, 16)

            def root(b):
                tiles = slice(SEQ_TILES * b, SEQ_TILES * (b + 1))
                act.wait_ge(var_ready, SEQ_TILES * (b + 1))
                act.activation(std[:, tiles], mean_var[:, tiles, 1], ACT.Sqrt, bias=eps[:, 0:1]
                               ).then_inc(std_ready, 1)

            def empty(unit, into, shaped=lambda bank: bank):
                n = START.index(unit)
                act.wait_ge(s_full, n + 1)
                act.copy(into, shaped(banks[:, S_BANK + n % S_RING, :])).then_inc(s_act, 1)

            def turned(c):
                empty(("xT", c), xnT[:, BANK * c:BANK * (c + 1)])

            def values(c):
                b, t = c // 2, 4 * (c % 2)
                for_group = v_all[:, GB * b:GB * (b + 1), t:t + 4, :].rearrange("p g t w -> p t g w")
                empty(("v", c), for_group, lambda bank: bank.rearrange("p (t g w) -> p t g w", t=4, g=GB))

            def first_part(y):
                act.wait_ge(rot_ready, y + 1)
                if y >= 2:
                    act.wait_ge(parts_out[y % 2], 16 * PARTS * (y // 2))
                act.copy(parts[:, y % 2, 0, :], rotated[:, y % 2, :]).then_inc(part0, 1)

            def second_part(y):
                act.wait_ge(rest_ready, y + 1)
                act.copy(parts[:, y % 2, 1, :], rest[:, y % 2, :]).then_inc(part1, 1)

            def split(ys):
                for y in ys:
                    first_part(y)
                    second_part(y)

            act.wait_ge(eps_set, 1)
            root(0)
            turned(0)
            turned(1)
            split(range(0, 2))
            root(1)
            split(range(2, 4))
            values(0)
            values(1)
            turned(2)
            turned(3)
            split(range(4, 8))
            values(2)
            values(3)

            act.wait_ge(b_in, 32)
            for kind, c, *f in FFN_ORDER:
                if kind == "up":
                    n = START.index((kind, c, *f))
                    act.wait_ge(s_full, n + 1)
                    if c >= 2:
                        act.wait_ge(s_full, START.index(("down", c - 2)) + 1)
                    act.activation(hT[:, c % 2, f[0], :], banks[:, S_BANK + n % S_RING, :], ACT.Gelu,
                                   bias=b1_sb[:, f[0]:f[0] + 1]).then_inc(s_act, 1)

            def outputs(i, r, half):
                g = 3 * i + r
                act.wait_ge(pv_done, STEPS * g + LAST_STEP[half] + 1)
                if not is_first(i, r):
                    act.wait_ge(a_full, (ring_at(i, r, "out1") if half else ring_at(i, r - 1, "out0")) + 1)
                act.copy(o_T[:, half, :], banks[:, O_BANK + half, :]).then_inc(o_out, 1)

            def turn(i, r):
                g = 3 * i + r
                for t in range(STEPS):
                    n = col_unit(t)[2]
                    if t >= P_RING or not is_first(i, r):
                        act.wait_ge(pv_done, STEPS * g + t - P_RING + 1)
                    for h in range(GH):
                        act.wait_ge(b_full, GH * (STEPS * g + t) + h + 1)
                        act.activation(probs[:, t % P_RING, h, 0:n], banks[:, B_BANK + h % B_RING, 0:n],
                                       ACT.Exp, scale=SCALE).then_inc(exp_done, 1)
                    if t == 2 and not is_first(i, r):
                        outputs(i, r - 1, 1)
                    if t == 6:
                        outputs(i, r, 0)

            turn(0, 0)
            with act.Fori(0, (GROUPS - 2) // 3) as i:
                for r in (1, 2, 3):
                    turn(i, r)
            turn(0, GROUPS - 1)
            outputs(0, GROUPS - 1, 1)
            for u in range(4):
                act.wait_ge(t_full, u + 1)
                act.copy(attnT[:, u, :], banks[:, A_BANK + u, :]).then_inc(t_copied, 1)

        @block.tensor
        def _(pe):
            def claim(n):
                if n >= S_RING:
                    who, count = emptied(n - S_RING)
                    pe.wait_ge(s_act if who == "act" else s_dve, count)
                return banks[:, S_BANK + n % S_RING, :]

            def start_unit(unit):
                bank = claim(START.index(unit))
                kind, c = unit[0], unit[1] if len(unit) > 1 else None
                if kind == "xT":
                    pe.wait_ge(xn_ready, 4 * (c + 1))
                    for t in range(4):
                        last = pe.transpose(bank[:, P * t:P * (t + 1)], xn[:, 4 * c + t, :], ident[:, :])
                elif kind == "proj":
                    z = unit[2]
                    pe.wait_ge(s_act, emptied(START.index(("xT", c)))[1])
                    w = (wqkv_sb, wswap_sb)[z % 2][:, D * (z // 2):D * (z // 2 + 1)]
                    last = pe.matmul(bank, w, xnT[:, BANK * c:BANK * (c + 1)], start=True, stop=True)
                elif kind == "v":
                    for t in range(4):
                        last = pe.matmul(bank[:, P * t:P * (t + 1)], xnT[:, BANK * c + P * t:BANK * c + P * (t + 1)],
                                         wqkv_sb[:, 2 * D:3 * D], start=True, stop=True)
                elif kind == "scale":
                    pe.wait_ge(wsum_ready, 2)
                    last = pe.matmul(bank[:, 0:2], ones[:, :], w_sums[:, :], start=True, stop=True)
                elif kind == "up":
                    pe.wait_ge(wt_ready, 1)
                    last = pe.matmul(bank, w1_t[:, P * unit[2]:P * (unit[2] + 1)], xnT[:, BANK * c:BANK * (c + 1)],
                                     start=True, stop=True)
                else:
                    pe.wait_ge(wt_ready, 2)
                    pe.wait_ge(s_act, emptied(START.index(("up", c, FF // P - 1)))[1])
                    for t in range(4):
                        for f in range(FF // P):
                            last = pe.matmul(bank[:, P * t:P * (t + 1)], hT[:, c % 2, f, P * t:P * (t + 1)],
                                             w2_t[:, f, :], start=(f == 0), stop=(f == FF // P - 1))
                last.then_inc(s_full, 1)

            def tile_of(op, rows, tile, h):
                at = P * (tile % 4)
                return op[0:rows, tile // 4, h, at:at + P]

            def rows(slot, i, r, t, h):
                tile, key, n, _ = row_unit(t)
                s = r % SLOTS
                if t == 0 and h == 0:
                    pe.wait_ge(op_in[s], OP_DMAS * (i + r // 3 + 1))
                pe.matmul(banks[:, A_BANK + slot, 0:n], tile_of(q_op[s], A_ROWS, tile, h),
                          k_op[s][0:A_ROWS, key // BANK, h, 0:n], start=True, stop=True).then_inc(a_full, 1)

            def cols(i, r, t, h):
                g, s = 3 * i + r, r % SLOTS
                tile, query, n, diagonal = col_unit(t)
                if t in (0, 4) and h == 0:
                    half = chunk_of(t)
                    pe.wait_ge(max_in[half], 16 * PARTS * (g + 1))
                if not (is_first(i, r) and t == 0 and h < B_RING):
                    pe.wait_ge(exp_done, GH * (STEPS * g + t) + h - B_RING + 1)
                last = pe.matmul(banks[:, B_BANK + h % B_RING, 0:n], tile_of(k_op[s], B_ROWS, tile, h),
                                 q_op[s][0:B_ROWS, query // BANK, h, BANK - n:BANK], start=True, stop=not diagonal)
                if diagonal:
                    last = pe.matmul(banks[:, B_BANK + h % B_RING, 0:P], ident_b[:, :], future[:, :],
                                     start=False, stop=True)
                last.then_inc(b_full, 1)

            def products(i, r, t):
                g, s = 3 * i + r, r % SLOTS
                tile, _, n, _ = col_unit(t)
                half = chunk_of(t)
                if t == 0:
                    pe.wait_ge(v_ready, g + 1)
                if t in (0, 4) and not is_first(i, r):
                    pe.wait_ge(o_out, 2 * g + half - 1)
                pe.wait_ge(exp_done, GH * (STEPS * g + t + 1))
                for h in range(GH):
                    last = pe.matmul(banks[32 * h:32 * (h + 1), O_BANK + half, BANK - n:BANK],
                                     v_op[s][:, tile, h, :], probs[:, t % P_RING, h, 0:n],
                                     start=(t in (0, 4)), stop=(t in LAST_STEP))
                last.then_inc(pv_done, 1)

            def maxima_up(slot, i, r, half):
                pe.wait_ge(max_split, 9 * (3 * i + r) + (9 if half else 4))
                pe.sem_inc(apart, 1)
                pe.transpose(banks[0:PARTS * GH * 4, A_BANK + slot, :].bitcast(BF16)[:, 0:P],
                             max_parts[:, half, :, :].rearrange("p a n -> p (a n)"),
                             ident_b[:, :]).then_inc(a_full, 1)

            def outputs_up(slot, i, r, half):
                pe.wait_ge(o_out, 2 * (3 * i + r) + half + 1)
                for t in range(4):
                    last = pe.transpose(banks[:, A_BANK + slot, P * t:P * (t + 1)],
                                        o_T[:, half, P * t:P * (t + 1)], ident[:, :])
                last.then_inc(a_full, 1)

            def turn(i, r):
                first, units = ring_base(i, r), turn_units(i, r)

                def pass_ring(t, place, head=None):
                    for u, (at, where, kind, h) in enumerate(units):
                        if (at, where) != (t, place) or h != head:
                            continue
                        slot = (ring_const(i, r) + u) % A_RING
                        pe.wait_ge(a_free, first + u - A_RING + 1)
                        if kind == "rows":
                            rows(slot, i, r + 1, t, h)
                        elif kind == "max1":
                            maxima_up(slot, i, r, 1)
                        elif kind == "max0":
                            maxima_up(slot, i, r + 1, 0)
                        elif kind == "out1":
                            outputs_up(slot, i, r - 1, 1)
                        else:
                            outputs_up(slot, i, r, 0)

                for t in range(STEPS):
                    pass_ring(t, "before")
                    for h in range(GH):
                        cols(i, r, t, h)
                        pass_ring(t, "beside", h)
                    pass_ring(t, "after")
                    if t >= 2:
                        products(i, r, t - 2)
                    elif not is_first(i, r):
                        products(i, r - 1, t + STEPS - 2)

            pe.wait_ge(pool_const, 5)
            pe.wait_ge(wqk_in, 32)
            for unit in EARLY + FFN_ORDER[:4]:
                start_unit(unit)
            ffn = list(FFN_ORDER[4:])
            pe.wait_ge(rows_in, 2 * SLOTS * 16)
            pe.wait_ge(pool_const, 11)
            for t in range(STEPS):
                if t == 5:
                    pe.wait_ge(a_free, GH * 5 - A_RING + 1)
                    maxima_up(GH * 5 % A_RING, 0, 0, 0)
                for h in range(GH):
                    u = GH * t + h + (t >= 5)
                    if u >= A_RING:
                        pe.wait_ge(a_free, u - A_RING + 1)
                    rows(u % A_RING, 0, 0, t, h)
                for _ in range(FFN_AFTER[t]):
                    start_unit(ffn.pop(0))
            pe.wait_ge(s_act, sum(EMPTIED_BY[u[0]] == "act" for u in START))
            pe.wait_ge(s_dve, sum(EMPTIED_BY[u[0]] == "dve" for u in START))

            turn(0, 0)
            with pe.Fori(0, (GROUPS - 2) // 3) as i:
                for r in (1, 2, 3):
                    turn(i, r)
            turn(0, GROUPS - 1)
            products(0, GROUPS - 1, STEPS - 2)
            products(0, GROUPS - 1, STEPS - 1)
            end = ring_base(0, GROUPS - 1) + len(LAST_TURN)
            pe.wait_ge(a_free, end - A_RING + 1)
            outputs_up(end % A_RING, 0, GROUPS - 1, 1)

            pe.wait_ge(a_free, end + 1)
            pe.wait_ge(wffn_in, 48)
            for u in range(4):
                for t in range(4 * u, 4 * u + 4):
                    b, tile = t // SEQ_TILES, t % SEQ_TILES
                    last = pe.transpose(banks[:, A_BANK + u, P * (t % 4):P * (t % 4 + 1)],
                                        attn[:, tile, GB * b:GB * (b + 1), :].rearrange("p g w -> p (g w)"), ident[:, :])
                last.then_inc(t_full, 1)
            for u in range(4):
                pe.wait_ge(t_copied, u + 1)
                for t in range(4):
                    last = pe.matmul(banks[:, B_BANK + u, P * t:P * (t + 1)], attnT[:, u, P * t:P * (t + 1)],
                                     wo_sb[:, :], start=True, stop=True)
                last.then_inc(y_full, 1)
    return nc


def kernel(L0_attn_x, L0_attn_w_qkv, L0_attn_w_out, L0_ffn_W1, L0_ffn_b1, L0_ffn_W2, L0_ffn_b2):
    import numpy as np
    import concourse.bacc as bacc
    from concourse.bass_utils import run_bass_kernel_spmd

    wqkv = np.ascontiguousarray(np.asarray(L0_attn_w_qkv).T)
    wswap = np.ascontiguousarray(wqkv[:, :2 * D].reshape(D, 2 * HEADS, 2, HD // 2)[:, :, ::-1, :].reshape(D, 2 * D))
    wo = np.ascontiguousarray(np.asarray(L0_attn_w_out).T)
    w1 = np.ascontiguousarray(np.asarray(L0_ffn_W1).T)
    w2 = np.ascontiguousarray(np.asarray(L0_ffn_W2).T.reshape(FF // P, P, D).transpose(1, 0, 2))
    b1 = np.ascontiguousarray(np.asarray(L0_ffn_b1).reshape(FF // P, P).T)
    b2 = np.ascontiguousarray(np.asarray(L0_ffn_b2).reshape(1, D))

    half = HD // 2
    inv_freq = (1.0 / np.float32(10000.0) ** (np.arange(half, dtype=np.float32) / half)).astype(np.float32)
    freqs = np.arange(SEQ, dtype=np.float32)[None, :] * inv_freq[:, None]
    cos = np.tile(np.cos(freqs).astype(np.float32), (2 * HEADS, 1))
    sin = np.tile(np.concatenate([-np.sin(freqs), np.sin(freqs)]).astype(np.float32), (HEADS, 1))

    const_rows = np.zeros((B_ROWS - PAIRS, 2 * GH * BANK), mybir.dt.np(BF16))
    const_rows[A_ROWS - PAIRS:] = -1

    arrays = {"x": np.ascontiguousarray(L0_attn_x), "wqkv": wqkv, "wswap": wswap, "wo": wo, "w1": w1, "b1": b1,
              "w2": w2, "b2": b2, "cos": cos, "sin": sin, "const_rows": const_rows}
    nc = bacc.Bacc("TRN2", target_bir_lowering=False, num_devices=1)
    args = {name: nc.dram_tensor(name, a.shape, mybir.dt.from_np(a.dtype), kind="ExternalInput").ap()
            for name, a in arrays.items()}
    out = nc.dram_tensor("out", (BATCH, SEQ, D), F32, kind="ExternalOutput").ap()
    build(nc, out=out, **args)
    return run_bass_kernel_spmd(nc, [arrays], core_ids=[0]).results[0]["out"]
```

```python
from contextlib import ExitStack

import concourse.bass as bass
from concourse import mybir

F32 = mybir.dt.float32
BF16 = mybir.dt.bfloat16
ALU = mybir.AluOpType
ACT = mybir.ActivationFunctionType
AX = mybir.AxisListType

P = 128
BANK = 512
BATCH, SEQ, D = 2, 1024, 128
HEADS, HD = 16, 8
FF = 512
TOK = BATCH * SEQ
TILES = TOK // P
CHUNKS = TOK // BANK
SEQ_TILES = SEQ // P
GH = 4
GROUPS = BATCH * HEADS // GH
GB = HEADS // GH
GW = GH * HD
PARTS = 3
PAIRS = PARTS * PARTS * HD
A_ROWS = 96
B_ROWS = A_ROWS + PARTS
STEPS = 12
A_RING, B_RING, P_RING, S_RING, SLOTS = 4, 2, 3, 4, 3
BIG = 3.0e38
SCALE = float(HD) ** -0.5
EPS = 1e-5


def row_unit(t):
    if t < 4:
        return 3 - t, 0, P * (4 - t), True
    if t % 2 == 0:
        return 4 + (t - 4) // 2, 0, BANK, False
    return 7 - (t - 5) // 2, BANK, P * (4 - (t - 5) // 2), True


def col_unit(t):
    if t < 4:
        return t, P * t, BANK - P * t, True
    if t % 2 == 0:
        return (t - 4) // 2, BANK, BANK, False
    d = (t - 5) // 2
    return 4 + d, BANK + P * d, BANK - P * d, True


def heads_of(t):
    together = max(1, BANK // col_unit(t)[2])
    together = 1 if together * col_unit(t)[2] > BANK else together
    return [tuple(range(h, h + together)) for h in range(0, GH, together)]


B_BEFORE = [sum(len(heads_of(s)) for s in range(t)) for t in range(STEPS + 1)]
B_UNITS = B_BEFORE[STEPS]
assert B_UNITS % B_RING == 0


def chunk_of(t):
    return 0 if t < 4 else 1


LAST_STEP = (3, 11)


LAST_TURN_EXTRA = [(1, "turn", 0), (2, "project", 0), (3, "turn", 1), (4, "project", 1),
                   (9, "turn", 2), (10, "project", 2)]


def ring_units(first, last):
    units = []
    for t in range(STEPS):
        if t == 8:
            units.append((t, "before", "out0", None))
        if t == 5 and not last:
            units.append((t, "before", "max0", None))
        if t == 4 and not first:
            units.append((t, "before", "out1", None))
        if not last:
            units += [(t, "beside", "rows", h) for h in range(GH)]
        if t == 0:
            units.append((t, "after", "max1", None))
        if last:
            units += [(t, "after", kind, u) for at, kind, u in LAST_TURN_EXTRA if at == t]
    return units


FIRST_TURN = ring_units(True, False)
TURN = ring_units(False, False)
LAST_TURN = ring_units(False, True)
PROLOGUE_UNITS = STEPS * GH + 1


def turn_units(i, r):
    return FIRST_TURN if is_first(i, r) else LAST_TURN if is_last(i, r) else TURN


def is_first(i, r):
    return isinstance(i, int) and 3 * i + r == 0


def is_last(i, r):
    return isinstance(i, int) and 3 * i + r == GROUPS - 1


def ring_base(i, r):
    if is_first(i, r):
        return PROLOGUE_UNITS
    return PROLOGUE_UNITS + len(FIRST_TURN) - len(TURN) + len(TURN) * r + 3 * len(TURN) * i


def ring_const(i, r):
    if is_first(i, r):
        return PROLOGUE_UNITS % A_RING
    return (PROLOGUE_UNITS + len(FIRST_TURN)) % A_RING


assert len(TURN) % A_RING == 0


def ring_at(i, r, kind, arg=None):
    return ring_base(i, r) + next(n for n, u in enumerate(turn_units(i, r)) if u[2:] == (kind, arg))


def max_at(i, r, half):
    if half:
        return ring_at(i, r, "max1") + (not isinstance(i, int) and r == 0)
    if is_first(i, r):
        return GH * 5
    return ring_at(i, r - 1, "max0")


ORDER = {4: ("B0", "B1", "A0", "A1", "A2", "B2", "A3", "B3"), 2: ("B0", "B1", "A0", "A1", "A2", "A3"),
         1: ("B0", "A0", "A1", "A2", "A3")}

WAY_IN = ([("xT", 0), ("xT", 1)] + [("proj", c, z) for c in (0, 1) for z in range(4)] + [("v", 0), ("v", 1)])
UPS = [[("up", c, f) for f in range(FF // P)] for c in range(CHUNKS)]
BEFORE_A = UPS[0] + UPS[1] + [("down", 0), ("xT", 2), ("xT", 3), ("down", 1)]
AFTER_STEP = [[("proj", 2, 0), ("proj", 2, 1)], [("proj", 2, 2), ("proj", 2, 3)],
              [("proj", 3, 0), ("proj", 3, 1)], [("proj", 3, 2), ("proj", 3, 3)],
              [("v", 2), ("v", 3)], UPS[2][:2], UPS[2][2:], UPS[3][:2], UPS[3][2:], [("down", 2)], [],
              [("down", 3)]]
REST = [("scale",)] + BEFORE_A + [u for units in AFTER_STEP for u in units]
EMPTIED_BY = {"xT": "act", "proj": "dve", "v": "act", "scale": "dve", "up": "act", "down": "dve"}


def place_of(unit):
    return (0, WAY_IN.index(unit)) if unit in WAY_IN else (1, REST.index(unit))


def emptied(ring, n):
    units = (WAY_IN, REST)[ring]
    who = EMPTIED_BY[units[n][0]]
    return who, sum(EMPTIED_BY[u[0]] == who for u in units[:n + 1])


def all_emptied(ring, who):
    return sum(EMPTIED_BY[u[0]] == who for u in (WAY_IN, REST)[ring])


def build(nc, x, wqkv, wswap, wo, w1, b1, w2, b2, cos, sin, const_rows, out):
    q_scratch, k_scratch = (nc.dram_tensor(name, (PARTS, HD, 2, GROUPS * GH, BANK), BF16, kind="Internal").ap()
                            for name in ("q_parts", "k_parts"))
    scratch = (q_scratch, k_scratch)

    with ExitStack() as ctx:
        def sb(name, shape, dt=F32):
            return ctx.enter_context(nc.sbuf_tensor(name, shape, dt))

        def sem(name):
            return ctx.enter_context(nc.semaphore(name))

        banks = ctx.enter_context(nc.psum_tensor("banks", [P, 8, BANK], F32))
        A_BANK, B_BANK, O_BANK = 0, 4, 6
        START_BANK = (0, 4)

        x_sb = sb("x_sb", [P, TILES, D])
        xn = sb("xn", [P, TILES, D])
        xnT = sb("xnT", [P, TOK])
        stats = sb("stats", [P, TILES, 6])
        mean_var = sb("mean_var", [P, TILES, 2])
        std = sb("std", [P, TILES])
        rstd = sb("rstd", [P, TILES])
        eps = sb("eps", [P, 1])
        warm = sb("warm", [P, 1])
        wqkv_sb = sb("wqkv_sb", [P, 3 * D])
        wswap_sb = sb("wswap_sb", [P, 2 * D])
        wo_sb = sb("wo_sb", [P, D])
        w1_sb = sb("w1_sb", [P, FF])
        w1_t = sb("w1_t", [P, FF])
        w2_sb = sb("w2_sb", [P, FF // P, D])
        w2_t = sb("w2_t", [P, FF // P, D])
        b1_sb = sb("b1_sb", [P, FF // P])
        b2_sb = sb("b2_sb", [P, D])
        w_sums = sb("w_sums", [P, 2])
        limit = sb("limit", [P, 2])
        neg_limit = sb("neg_limit", [P, 2])
        below = sb("below", [P, FF])
        above = sb("above", [P, FF])
        newton = sb("newton", [P, 2, TILES])
        cos_sb = sb("cos_sb", [P, SEQ])
        sin_sb = sb("sin_sb", [P, SEQ])
        ident = sb("ident", [P, P])
        ident_b = sb("ident_b", [P, P], BF16)
        ones = sb("ones", [P, P])
        causal = sb("causal", [P, BANK])
        future = sb("future", [P, P], BF16)
        parts = sb("parts", [P, 4, PARTS, BANK], BF16)
        hT = sb("hT", [P, 2, FF // P, BANK])
        base = sb("base", [P, TILES, D])
        v_all = sb("v_all", [P, GROUPS, SEQ_TILES, GW])
        q_op = [sb(f"q_op{s}", [P, 2, GH, BANK], BF16) for s in range(SLOTS)]
        k_op = [sb(f"k_op{s}", [P, 2, GH, BANK], BF16) for s in range(SLOTS)]
        v_op = [sb(f"v_op{s}", [P, SEQ_TILES, GH, 32]) for s in range(SLOTS)]
        junk = sb("junk", [P, A_RING, BANK], BF16)
        maxima = sb("maxima", [P, 3, GH, 4])
        max_rest = sb("max_rest", [P, 2, GH * 4])
        max_parts = sb("max_parts", [P, 2, PARTS, GH * 4], BF16)
        max_rows = sb("max_rows", [PARTS * GH * 4, 2, P], BF16)
        probs = sb("probs", [P, P_RING, GH, BANK])
        start_room = probs[:, :, :, :].rearrange("p s h n -> p (s h n)")
        rotated = start_room[:, 0:4 * BANK].rearrange("p (y n) -> p y n", y=4)
        rest = start_room[:, 4 * BANK:8 * BANK].rearrange("p (y n) -> p y n", y=4)
        rot_a = start_room[:, 8 * BANK:10 * BANK].rearrange("p (y n) -> p y n", y=2)
        rot_b = start_room[:, 10 * BANK:12 * BANK].rearrange("p (y n) -> p y n", y=2)
        o_T = sb("o_T", [P, 2, BANK])
        recip = sb("recip", [P, 2, 4, GH])
        attn = sb("attn", [P, SEQ_TILES, GROUPS, GW])
        attnT = xnT[:, :].rearrange("p (u n) -> p u n", u=4)
        result = x_sb[:, :, :].rearrange("p (u t) d -> p u (t d)", u=4)

        x_in = [sem(f"x_in{c}") for c in range(CHUNKS)]
        wqk_in, w1_in, wo_in, b_in, table_in = sem("wqk_in"), sem("w1_in"), sem("wo_in"), sem("b_in"), sem("table_in")
        act_step = sem("act_step")
        pool_const = sem("pool_const")
        rows_in = sem("rows_in")
        dve_step = sem("dve_step")
        apart = sem("apart")
        pool_step = sem("pool_step")
        eps_set, var_ready, std_ready, xn_ready = sem("eps_set"), sem("var_ready"), sem("std_ready"), sem("xn_ready")
        limit_ready = sem("limit_ready")
        wsum_ready, wt_ready = sem("wsum_ready"), sem("wt_ready")
        start_full = [sem("way_in_full"), sem("rest_full")]
        start_emptied = [{"act": sem("way_in_act"), "dve": sem("way_in_dve")},
                         {"act": sem("rest_act"), "dve": sem("rest_dve")}]
        rot_ready, part0, part1 = sem("rot_ready"), sem("part0"), sem("part1")
        rest_ready = {"pool": sem("rest_pool"), "dve": sem("rest_dve_")}
        part2 = {"pool": sem("part2_pool"), "dve": sem("part2_dve")}
        parts_out = [sem(f"parts_out{b}") for b in range(BATCH)]
        xb_ready = sem("xb_ready")
        op_in = [sem(f"op_in{s}") for s in range(SLOTS)]
        v_ready = sem("v_ready")
        a_full, a_free = sem("a_full"), sem("a_free")
        max_split = sem("max_split")
        max_in = [sem("max_in0"), sem("max_in1")]
        b_full, exp_done = sem("b_full"), sem("exp_done")
        pv_done = sem("pv_done")
        o_out = sem("o_out")
        recip_ready = sem("recip_ready")
        out_done = sem("out_done")

        block = ctx.enter_context(nc.Block())
        x_tiles = x.rearrange("b (t p) d -> p (b t) d", p=P)
        out_tiles = out.rearrange("b (t p) d -> p (b t) d", p=P)

        def start_bank(unit):
            ring, n = place_of(unit)
            return banks[:, START_BANK[ring] + n % S_RING, :]

        def filled(eng, unit):
            ring, n = place_of(unit)
            eng.wait_ge(start_full[ring], n + 1)

        def wait_emptied(eng, unit):
            ring, n = place_of(unit)
            who, count = emptied(ring, n)
            eng.wait_ge(start_emptied[ring][who], count)

        splitter = ["pool", "dve", "pool", "dve", "pool", "pool", "pool", "pool"]
        nth = [splitter[:y + 1].count(splitter[y]) for y in range(8)]

        def store_parts(eng, y):
            c, z = y // 2, y % 2
            eng.wait_ge(part2[splitter[y]], nth[y])
            b, half = c // 2, c % 2
            for a in range(PARTS):
                eng.dma_start(scratch[z][a, :, half, HEADS * b:HEADS * (b + 1), :].rearrange("d h n -> h d n"),
                              parts[:, y % 4, a, :]).then_inc(parts_out[b], 16)

        def load_ops(eng, i, r):
            g, s = 3 * i + r, r % SLOTS

            def load(op, source, row, part, parts_n):
                src = source[part:part + parts_n, :, :, bass.ts(g, GH), :].rearrange("a d c h n -> (a d) c (h n)")
                dst = op[HD * row:HD * (row + parts_n), :, :, :].rearrange("p c h n -> p c (h n)")
                eng.dma_start(dst, src).then_inc(op_in[s], 16)

            for u in range(PARTS):
                load(k_op[s], k_scratch, PARTS * u, 0, PARTS)
                load(q_op[s], q_scratch, PARTS * u, u, PARTS - u)
                if u:
                    load(q_op[s], q_scratch, PARTS * u + PARTS - u, 0, u)

        OP_DMAS = 16 * (3 * PARTS - 1)

        END = ring_base(0, GROUPS - 1) + len(LAST_TURN)

        def project_at(u):
            return END + 2 if u == 3 else ring_at(0, GROUPS - 1, "project", u)

        def load_max(eng, i, r, half):
            g, s = 3 * i + r, r % SLOTS
            eng.wait_ge(a_free, max_at(i, r, half) + 1)
            for a in range(PARTS):
                eng.dma_start(q_op[s][A_ROWS + a:A_ROWS + a + 1, half, :, :].rearrange("o h (i n) -> o (h i) n", n=P),
                              max_rows[16 * a:16 * a + 16, half, :]).then_inc(max_in[half], 16)

        @block.sync
        def _(sp):
            for c in range(CHUNKS):
                sp.dma_start(x_sb[:, 4 * c:4 * c + 4, :], x_tiles[:, 4 * c:4 * c + 4, :]).then_inc(x_in[c], 16)
            sp.dma_start(cos_sb[:, :], cos).then_inc(table_in, 16)
            sp.dma_start(sin_sb[:, :], sin).then_inc(table_in, 16)
            for s in range(SLOTS):
                sp.dma_start(q_op[s][PAIRS:A_ROWS, :, :, :].rearrange("p c h n -> p (c h n)"),
                             const_rows[0:A_ROWS - PAIRS, :]).then_inc(rows_in, 16)
                sp.dma_start(k_op[s][PAIRS:B_ROWS, :, :, :].rearrange("p c h n -> p (c h n)"),
                             const_rows).then_inc(rows_in, 16)
            for y in range(4):
                store_parts(sp, y)
            sp.wait_ge(parts_out[0], 16 * PARTS * 4)
            load_ops(sp, 0, 0)
            load_ops(sp, 0, 1)
            load_max(sp, 0, 0, 0)
            for y in range(4, 8):
                store_parts(sp, y)
            sp.wait_ge(parts_out[1], 16 * PARTS * 4)

            def turn(i, r):
                g = 3 * i + r
                if not (isinstance(i, int) and g + 2 >= GROUPS):
                    sp.wait_ge(b_full, B_UNITS * g + 1)
                    load_ops(sp, i, r + 2)
                load_max(sp, i, r, 1)
                if not is_last(i, r):
                    load_max(sp, i, r + 1, 0)

            with sp.Fori(0, (GROUPS - 2) // 3) as i:
                for r in range(3):
                    turn(i, r)
            turn(0, GROUPS - 2)
            turn(0, GROUPS - 1)
            for u in range(4):
                sp.wait_ge(a_free, project_at(u) + 1)
                sp.dma_start(out_tiles[:, 4 * u:4 * u + 4, :],
                             result[:, u, :].rearrange("p (t d) -> p t d", d=D)).then_inc(out_done, 16)
            sp.wait_ge(out_done, 64)

        @block.gpsimd
        def _(pool):
            pool.memset(ident[:, :], 0.0).then_inc(pool_step, 1)
            pool.memset(causal[:, :], 0.0).then_inc(pool_step, 1)
            pool.memset(future[:, :], 0.0).then_inc(pool_step, 1)
            pool.memset(ones[:, :], 1.0).then_inc(pool_const, 1)
            pool.wait_ge(pool_step, 3)
            pool.affine_select(out=ident[:, :], in_=ident[:, :], compare_op=ALU.not_equal, fill=1.0, base=0,
                               pattern=[[-1, P]], channel_multiplier=1).then_inc(pool_const, 1)
            pool.affine_select(out=future[:, :], in_=future[:, :], compare_op=ALU.is_ge, fill=-BIG, base=0,
                               pattern=[[1, P]], channel_multiplier=-1).then_inc(pool_const, 1)
            pool.affine_select(out=causal[:, BANK - P:BANK], in_=causal[:, BANK - P:BANK], compare_op=ALU.is_ge,
                               fill=-BIG, base=0, pattern=[[-1, P]], channel_multiplier=1).then_inc(pool_const, 1)
            pool.wait_ge(pool_const, 4)
            pool.tensor_copy(ident_b[:, :], ident[:, :]).then_inc(pool_const, 1)
            for s in range(SLOTS):
                pool.memset(v_op[s][:, :, :, HD:32], 0.0).then_inc(pool_const, 1)
            pool.wait_ge(pool_const, 8)
            for s in range(SLOTS):
                pool.memset(v_op[s][:, :, :, HD:HD + 1], 1.0).then_inc(pool_const, 1)

            pool.wait_ge(limit_ready, 2)
            for k, (w, w_t) in enumerate(((w1_sb[:, :], w1_t[:, :]),
                                          (w2_sb[:, :, :].rearrange("p f d -> p (f d)"),
                                           w2_t[:, :, :].rearrange("p f d -> p (f d)")))):
                pool.tensor_scalar(below[:, :], w, neg_limit[:, k:k + 1], None, ALU.is_lt).then_inc(pool_step, 1)
                pool.tensor_scalar(above[:, :], w, limit[:, k:k + 1], None, ALU.is_gt).then_inc(pool_step, 1)
                pool.wait_ge(pool_step, 3 + 2 * (k + 1))
                pool.tensor_tensor(w_t, above[:, :], below[:, :], ALU.subtract).then_inc(wt_ready, 1)
                pool.wait_ge(wt_ready, k + 1)

            def split_rest(y):
                pool.wait_ge(part0, y + 1)
                pool.tensor_tensor(rest[:, y % 4, :], rotated[:, y % 4, :], parts[:, y % 4, 0, :],
                                   ALU.subtract).then_inc(rest_ready["pool"], 1)

            def split_last(y):
                pool.wait_ge(part1, y + 1)
                pool.tensor_tensor(parts[:, y % 4, 2, :], rest[:, y % 4, :], parts[:, y % 4, 1, :],
                                   ALU.subtract).then_inc(part2["pool"], 1)

            for y in (0, 2):
                split_rest(y)
                split_last(y)
            for c in range(CHUNKS):
                pool.wait_ge(x_in[c], 16)
            pool.wait_ge(b_in, 32)
            pool.tensor_tensor(base[:, :, :], x_sb[:, :, :], b2_sb[:, :].unsqueeze(1).to_broadcast([P, TILES, D]),
                               ALU.add).then_inc(xb_ready, 1)
            for y in range(4, 8):
                split_rest(y)
                if y > 4:
                    split_last(y - 1)
            split_last(7)

            def fill_v(i, r):
                g, s = 3 * i + r, r % SLOTS
                pool.tensor_copy(v_op[s][:, :, :, 0:HD],
                                 v_all[:, g, :, :].rearrange("p t (h d) -> p t h d", d=HD)).then_inc(v_ready, 1)

            def turn(i, r):
                if not is_first(i, r):
                    pool.wait_ge(pv_done, STEPS * (3 * i + r - 1))
                    pool.sem_inc(apart, 1)
                fill_v(i, r + 1)

            wait_emptied(pool, ("v", 1))
            fill_v(0, 0)
            wait_emptied(pool, ("v", 3))
            turn(0, 0)
            with pool.Fori(0, (GROUPS - 2) // 3) as i:
                for r in (1, 2, 3):
                    turn(i, r)

        @block.vector
        def _(dve):
            own = [0]

            def mark(instruction):
                own[0] += 1
                instruction.then_inc(dve_step, 1)
                return own[0]

            dve.memset(eps[:, :], EPS).then_inc(eps_set, 1)

            def statistics(c):
                dve.wait_ge(x_in[c], 16)
                for t in range(4 * c, 4 * c + 4):
                    last = mark(dve.bn_stats(stats[:, t, :], x_sb[:, t, :]))
                dve.wait_ge(dve_step, last)
                for t in range(4 * c, 4 * c + 4):
                    dve.bn_aggr(mean_var[:, t, :], stats[:, t, :]).then_inc(var_ready, 1)

            def normalise(c):
                tiles = slice(4 * c, 4 * c + 4)
                dve.wait_ge(std_ready, c + 1)
                dve.wait_ge(dve_step, mark(dve.reciprocal(rstd[:, tiles], std[:, tiles])))
                dve.wait_ge(dve_step, mark(dve.tensor_tensor(newton[:, 0, tiles], rstd[:, tiles], rstd[:, tiles],
                                                             ALU.mult)))
                dve.wait_ge(dve_step, mark(dve.scalar_tensor_tensor(
                    out=newton[:, 1, tiles], in0=mean_var[:, tiles, 1], scalar=EPS, in1=newton[:, 0, tiles],
                    op0=ALU.add, op1=ALU.mult)))
                dve.wait_ge(dve_step, mark(dve.tensor_scalar(newton[:, 0, tiles], newton[:, 1, tiles], -0.5, 1.5,
                                                             ALU.mult, ALU.add)))
                dve.wait_ge(dve_step, mark(dve.tensor_tensor(rstd[:, tiles], rstd[:, tiles], newton[:, 0, tiles],
                                                             ALU.mult)))
                for t in range(4 * c, 4 * c + 4):
                    dve.tensor_scalar(xn[:, t, :], x_sb[:, t, :], mean_var[:, t, 0:1], rstd[:, t:t + 1],
                                      ALU.subtract, ALU.mult).then_inc(xn_ready, 1)

            def rotate(y):
                c, z = y // 2, y % 2
                at = (c % 2) * BANK
                if y >= 4:
                    dve.wait_ge(part1, y - 3)
                for half, (buf, table) in enumerate(((rot_a, cos_sb), (rot_b, sin_sb))):
                    unit = ("proj", c, 2 * z + half)
                    ring, n = place_of(unit)
                    filled(dve, unit)
                    dve.tensor_tensor(buf[:, y % 2, :], start_bank(unit), table[:, at:at + BANK],
                                      ALU.mult).then_inc(start_emptied[ring]["dve"], 1)
                wait_emptied(dve, unit)
                dve.tensor_tensor(rotated[:, y % 4, :], rot_a[:, y % 2, :], rot_b[:, y % 2, :],
                                  ALU.add).then_inc(rot_ready, 1)

            def split_rest(y):
                dve.wait_ge(part0, y + 1)
                dve.tensor_tensor(rest[:, y % 4, :], rotated[:, y % 4, :], parts[:, y % 4, 0, :],
                                  ALU.subtract).then_inc(rest_ready["dve"], 1)

            def split_last(y):
                dve.wait_ge(part1, y + 1)
                dve.tensor_tensor(parts[:, y % 4, 2, :], rest[:, y % 4, :], parts[:, y % 4, 1, :],
                                  ALU.subtract).then_inc(part2["dve"], 1)

            dve.wait_ge(w1_in, 32)
            dve.tensor_reduce(w_sums[:, 0:1], w1_sb[:, :], AX.X, ALU.add,
                              apply_absolute_value=True).then_inc(wsum_ready, 1)
            dve.tensor_reduce(w_sums[:, 1:2], w2_sb[:, :, :], AX.XY, ALU.add,
                              apply_absolute_value=True).then_inc(wsum_ready, 1)
            statistics(0)
            statistics(1)
            normalise(0)
            normalise(1)
            filled(dve, ("scale",))
            dve.tensor_scalar(limit[:, :], start_bank(("scale",))[:, 0:2], 1.0 / (FF * D), 1e-8,
                              ALU.mult, ALU.max).then_inc(start_emptied[1]["dve"], 1)
            wait_emptied(dve, ("scale",))
            dve.tensor_scalar(neg_limit[:, :], limit[:, :], -0.5, None, ALU.mult).then_inc(limit_ready, 1)
            dve.wait_ge(limit_ready, 1)
            dve.tensor_scalar(limit[:, :], neg_limit[:, :], -1.0, None, ALU.mult).then_inc(limit_ready, 1)
            statistics(2)
            statistics(3)
            dve.wait_ge(table_in, 32)
            rotate(0)
            rotate(1)
            rotate(2)
            split_rest(1)
            rotate(3)
            split_last(1)
            split_rest(3)
            normalise(2)
            split_last(3)
            normalise(3)

            def add_ffn(c):
                if c == 0:
                    dve.wait_ge(xb_ready, 1)
                filled(dve, ("down", c))
                tile4 = base[:, 4 * c:4 * c + 4, :].rearrange("p t d -> p (t d)")
                dve.tensor_tensor(tile4, start_bank(("down", c)), tile4, ALU.add).then_inc(start_emptied[1]["dve"], 1)

            def rows(slot, t, h):
                i, _, n, diagonal = row_unit(t)
                scores = banks[:, A_BANK + slot, 0:n]
                which = 0 if t < 4 else 1 + t % 2
                into = maxima[:, which, h, i % 4:i % 4 + 1]
                if diagonal:
                    dve.tensor_tensor_reduce(junk[:, slot, 0:n], scores, causal[:, BANK - n:BANK], 1.0, -BIG,
                                             ALU.add, ALU.max, into).then_inc(a_free, 1)
                else:
                    dve.tensor_reduce(into, scores, AX.X, ALU.max).then_inc(a_free, 1)

            def split_max(i, r, half, emptied_units):
                done = 9 * (3 * i + r) + 4 * half
                first, upper, lower = (maxima[:, w, :, :].rearrange("p h i -> p (h i)") for w in range(3))
                whole = upper if half else first
                part = [max_parts[:, half, a, :] for a in range(PARTS)]
                dve.wait_ge(a_free, emptied_units)
                if half:
                    dve.tensor_tensor(upper, upper, lower, ALU.max).then_inc(max_split, 1)
                    done = done + 1
                    dve.wait_ge(max_split, done)
                dve.tensor_copy(part[0], whole).then_inc(max_split, 1)
                dve.wait_ge(max_split, done + 1)
                dve.tensor_tensor(max_rest[:, 0, :], whole, part[0], ALU.subtract).then_inc(max_split, 1)
                dve.wait_ge(max_split, done + 2)
                dve.tensor_copy(part[1], max_rest[:, 0, :]).then_inc(max_split, 1)
                dve.wait_ge(max_split, done + 3)
                dve.tensor_tensor(part[2], max_rest[:, 0, :], part[1], ALU.subtract).then_inc(max_split, 1)

            def copy_max(slot, i, r, half):
                g = 3 * i + r
                if not is_first(i, r):
                    dve.wait_ge(max_in[half], 16 * PARTS * g)
                rows_T = banks[0:PARTS * GH * 4, A_BANK + slot, :].bitcast(BF16)[:, 0:P]
                dve.tensor_copy(max_rows[:, half, :], rows_T).then_inc(a_free, 1)

            def divide(slot, i, r, half):
                g = 3 * i + r
                turned = banks[:, A_BANK + slot, :].rearrange("p (t h w) -> p t h w", t=4, h=GH)
                dve.reciprocal(recip[:, half, :, :], turned[:, :, :, HD]).then_inc(recip_ready, 1)
                dve.wait_ge(recip_ready, 2 * g + half + 1)
                into = attn[:, 4 * half:4 * half + 4, g, :].rearrange("p t (h d) -> p t h d", d=HD)
                dve.tensor_tensor(into, turned[:, :, :, 0:HD],
                                  recip[:, half, :, :].unsqueeze(3).to_broadcast([P, 4, GH, HD]),
                                  ALU.mult).then_inc(a_free, 1)

            def turn_all(slot, u):
                dve.tensor_copy(attnT[:, u, :], banks[:, A_BANK + slot, :]).then_inc(a_free, 1)

            def add_projection(slot, u):
                dve.tensor_tensor(result[:, u, :], banks[:, A_BANK + slot, :],
                                  base[:, 4 * u:4 * u + 4, :].rearrange("p t d -> p (t d)"),
                                  ALU.add).then_inc(a_free, 1)

            def turn(i, r):
                units = turn_units(i, r)
                first = ring_base(i, r)
                for u, (t, _, kind, h) in enumerate(units):
                    slot = (ring_const(i, r) + u) % A_RING
                    dve.wait_ge(a_full, first + u + 1)
                    if kind == "rows" and row_unit(t)[3]:
                        dve.sem_inc(apart, 1)
                    if kind == "rows":
                        rows(slot, t, h)
                    elif kind == "max1":
                        copy_max(slot, i, r, 1)
                    elif kind == "max0":
                        copy_max(slot, i, r + 1, 0)
                    elif kind == "out1":
                        divide(slot, i, r - 1, 1)
                    elif kind == "out0":
                        divide(slot, i, r, 0)
                    elif kind == "turn":
                        turn_all(slot, h)
                    else:
                        add_projection(slot, h)
                    if kind == "rows" and h == GH - 1 and t in LAST_STEP:
                        split_max(i, r + 1, LAST_STEP.index(t), first + u + 1)

            dve.wait_ge(pool_const, 4)
            add_ffn(0)
            add_ffn(1)
            for t in range(STEPS):
                if t == 5:
                    dve.wait_ge(a_full, GH * 5 + 1)
                    copy_max(GH * 5 % A_RING, 0, 0, 0)
                for h in range(GH):
                    u = GH * t + h + (t >= 5)
                    dve.wait_ge(a_full, u + 1)
                    rows(u % A_RING, t, h)
                if t in LAST_STEP:
                    split_max(0, 0, LAST_STEP.index(t), GH * (t + 1) + (t >= 5))
                for unit in AFTER_STEP[t]:
                    if unit[0] == "down":
                        add_ffn(unit[1])
                    elif unit[0] == "proj" and unit[2] % 2:
                        rotate(2 * unit[1] + unit[2] // 2)
            turn(0, 0)
            with dve.Fori(0, (GROUPS - 2) // 3) as i:
                for r in (1, 2, 3):
                    turn(i, r)
            turn(0, GROUPS - 1)
            dve.wait_ge(a_full, END + 1)
            divide(END % A_RING, 0, GROUPS - 1, 1)
            dve.wait_ge(a_full, END + 2)
            turn_all((END + 1) % A_RING, 3)
            dve.wait_ge(a_full, END + 3)
            add_projection((END + 2) % A_RING, 3)

        @block.scalar
        def _(act):
            act.dma_start(w1_sb[:, :], w1).then_inc(w1_in, 16)
            act.dma_start(w2_sb[:, :, :], w2).then_inc(w1_in, 16)
            act.dma_start(wqkv_sb[:, :], wqkv).then_inc(wqk_in, 16)
            act.dma_start(wswap_sb[:, :], wswap).then_inc(wqk_in, 16)
            act.dma_start(b1_sb[:, :], b1).then_inc(b_in, 16)
            act.dma_start(b2_sb[:, :], b2.to_broadcast([P, D])).then_inc(b_in, 16)
            act.dma_start(wo_sb[:, :], wo).then_inc(wo_in, 16)

            def root(c):
                tiles = slice(4 * c, 4 * c + 4)
                act.wait_ge(var_ready, 4 * (c + 1))
                act.activation(std[:, tiles], mean_var[:, tiles, 1], ACT.Sqrt, bias=eps[:, 0:1]
                               ).then_inc(std_ready, 1)

            def empty(unit, into, shaped=lambda bank: bank):
                filled(act, unit)
                act.copy(into, shaped(start_bank(unit))).then_inc(start_emptied[place_of(unit)[0]]["act"], 1)

            def turned(c):
                empty(("xT", c), xnT[:, BANK * c:BANK * (c + 1)])

            def values(c):
                b, t = c // 2, 4 * (c % 2)
                for_group = v_all[:, GB * b:GB * (b + 1), t:t + 4, :].rearrange("p g t w -> p t g w")
                empty(("v", c), for_group, lambda bank: bank.rearrange("p (t g w) -> p t g w", t=4, g=GB))

            def first_part(y):
                act.wait_ge(rot_ready, y + 1)
                if y >= 4:
                    act.wait_ge(parts_out[0], 16 * PARTS * 4)
                act.copy(parts[:, y % 4, 0, :], rotated[:, y % 4, :]).then_inc(part0, 1)

            def second_part(y):
                act.wait_ge(rest_ready[splitter[y]], nth[y])
                act.copy(parts[:, y % 4, 1, :], rest[:, y % 4, :]).then_inc(part1, 1)

            def gelu(c, f):
                filled(act, ("up", c, f))
                if c >= 2:
                    filled(act, ("down", c - 2))
                act.activation(hT[:, c % 2, f, :], start_bank(("up", c, f)), ACT.Gelu,
                               bias=b1_sb[:, f:f + 1]).then_inc(start_emptied[1]["act"], 1)

            act.wait_ge(eps_set, 1)
            act.activation(warm[:, :], eps[:, :], ACT.Sqrt).then_inc(act_step, 1)
            root(0)
            root(1)
            turned(0)
            turned(1)
            root(2)
            root(3)
            first_part(0)
            first_part(1)
            second_part(0)
            first_part(2)
            second_part(1)
            first_part(3)
            second_part(2)
            second_part(3)
            values(0)
            values(1)
            act.wait_ge(b_in, 32)
            for c in (0, 1):
                for f in range(FF // P):
                    gelu(c, f)
            turned(2)
            turned(3)
            for y in range(4, 8):
                first_part(y)
                if y > 4:
                    second_part(y - 1)
            second_part(7)
            values(2)
            values(3)
            for c in (2, 3):
                for f in range(FF // P):
                    gelu(c, f)
            act.wait_ge(part2["pool"], nth[7])
            act.wait_ge(rot_ready, 8)

            def outputs(i, r, half):
                g = 3 * i + r
                act.wait_ge(pv_done, STEPS * g + LAST_STEP[half] + 1)
                if not is_first(i, r):
                    act.wait_ge(a_full, (ring_at(i, r, "out1") if half else ring_at(i, r - 1, "out0")) + 1)
                act.copy(o_T[:, half, :], banks[:, O_BANK + half, :]).then_inc(o_out, 1)

            def turn(i, r):
                g = 3 * i + r
                for t in range(STEPS):
                    n = col_unit(t)[2]
                    if t >= P_RING or not is_first(i, r):
                        act.wait_ge(pv_done, STEPS * g + t - P_RING + 1)
                    for k, heads in enumerate(heads_of(t)):
                        unit = B_BEFORE[t] + k
                        act.wait_ge(b_full, B_UNITS * g + unit + 1)
                        scores = banks[:, B_BANK + unit % B_RING, 0:n * len(heads)]
                        act.activation(probs[:, t % P_RING, heads[0]:heads[-1] + 1, 0:n],
                                       scores.rearrange("p (h n) -> p h n", n=n), ACT.Exp,
                                       scale=SCALE).then_inc(exp_done, 1)
                    if t == 2 and not is_first(i, r):
                        outputs(i, r - 1, 1)
                    if t == 6:
                        outputs(i, r, 0)

            turn(0, 0)
            with act.Fori(0, (GROUPS - 2) // 3) as i:
                for r in (1, 2, 3):
                    turn(i, r)
            turn(0, GROUPS - 1)
            outputs(0, GROUPS - 1, 1)

        @block.tensor
        def _(pe):
            def start_unit(unit):
                ring, n = place_of(unit)
                if n >= S_RING:
                    who, count = emptied(ring, n - S_RING)
                    pe.wait_ge(start_emptied[ring][who], count)
                bank = start_bank(unit)
                kind, c = unit[0], unit[1] if len(unit) > 1 else None
                if kind == "xT":
                    pe.wait_ge(xn_ready, 4 * (c + 1))
                    for t in range(4):
                        last = pe.transpose(bank[:, P * t:P * (t + 1)], xn[:, 4 * c + t, :], ident[:, :])
                elif kind == "proj":
                    z = unit[2]
                    wait_emptied(pe, ("xT", c))
                    w = (wqkv_sb, wswap_sb)[z % 2][:, D * (z // 2):D * (z // 2 + 1)]
                    last = pe.matmul(bank, w, xnT[:, BANK * c:BANK * (c + 1)], start=True, stop=True)
                elif kind == "v":
                    for t in range(4):
                        last = pe.matmul(bank[:, P * t:P * (t + 1)], xnT[:, BANK * c + P * t:BANK * c + P * (t + 1)],
                                         wqkv_sb[:, 2 * D:3 * D], start=True, stop=True)
                elif kind == "scale":
                    pe.wait_ge(wsum_ready, 2)
                    last = pe.matmul(bank[:, 0:2], ones[:, :], w_sums[:, :], start=True, stop=True)
                elif kind == "up":
                    pe.wait_ge(wt_ready, 1)
                    last = pe.matmul(bank, w1_t[:, P * unit[2]:P * (unit[2] + 1)], xnT[:, BANK * c:BANK * (c + 1)],
                                     start=True, stop=True)
                else:
                    pe.wait_ge(wt_ready, 2)
                    wait_emptied(pe, ("up", c, FF // P - 1))
                    for t in range(4):
                        for f in range(FF // P):
                            last = pe.matmul(bank[:, P * t:P * (t + 1)], hT[:, c % 2, f, P * t:P * (t + 1)],
                                             w2_t[:, f, :], start=(f == 0), stop=(f == FF // P - 1))
                last.then_inc(start_full[ring], 1)

            def tile_of(op, rows, tile, h):
                at = P * (tile % 4)
                return op[0:rows, tile // 4, h, at:at + P]

            def rows(slot, i, r, t, h):
                tile, key, n, _ = row_unit(t)
                s = r % SLOTS
                if t == 0 and h == 0:
                    pe.wait_ge(op_in[s], OP_DMAS * (i + r // 3 + 1))
                pe.matmul(banks[:, A_BANK + slot, 0:n], tile_of(q_op[s], A_ROWS, tile, h),
                          k_op[s][0:A_ROWS, key // BANK, h, 0:n], start=True, stop=True).then_inc(a_full, 1)

            def cols(i, r, t, k):
                g, s = 3 * i + r, r % SLOTS
                tile, query, n, diagonal = col_unit(t)
                unit = B_BEFORE[t] + k
                if t in (0, 4) and k == 0:
                    pe.wait_ge(max_in[chunk_of(t)], 16 * PARTS * (g + 1))
                if not (is_first(i, r) and unit < B_RING):
                    pe.wait_ge(exp_done, B_UNITS * g + unit - B_RING + 1)
                bank = banks[:, B_BANK + unit % B_RING, :]
                for k, h in enumerate(heads_of(t)[k]):
                    last = pe.matmul(bank[:, n * k:n * (k + 1)], tile_of(k_op[s], B_ROWS, tile, h),
                                     q_op[s][0:B_ROWS, query // BANK, h, BANK - n:BANK],
                                     start=True, stop=not diagonal)
                    if diagonal:
                        last = pe.matmul(bank[:, n * k:n * k + P], ident_b[:, :], future[:, :],
                                         start=False, stop=True)
                last.then_inc(b_full, 1)

            def products(i, r, t):
                g, s = 3 * i + r, r % SLOTS
                tile, _, n, _ = col_unit(t)
                half = chunk_of(t)
                if t == 0:
                    pe.wait_ge(v_ready, g + 1)
                if t in (0, 4) and not is_first(i, r):
                    pe.wait_ge(o_out, 2 * g + half - 1)
                pe.wait_ge(exp_done, B_UNITS * g + B_BEFORE[t + 1])
                for h in range(GH):
                    last = pe.matmul(banks[32 * h:32 * (h + 1), O_BANK + half, BANK - n:BANK],
                                     v_op[s][:, tile, h, :], probs[:, t % P_RING, h, 0:n],
                                     start=(t in (0, 4)), stop=(t in LAST_STEP))
                last.then_inc(pv_done, 1)

            def maxima_up(slot, i, r, half):
                pe.wait_ge(max_split, 9 * (3 * i + r) + (9 if half else 4))
                pe.sem_inc(apart, 1)
                pe.transpose(banks[0:PARTS * GH * 4, A_BANK + slot, :].bitcast(BF16)[:, 0:P],
                             max_parts[:, half, :, :].rearrange("p a n -> p (a n)"),
                             ident_b[:, :]).then_inc(a_full, 1)

            def outputs_up(slot, i, r, half):
                pe.wait_ge(o_out, 2 * (3 * i + r) + half + 1)
                for t in range(4):
                    last = pe.transpose(banks[:, A_BANK + slot, P * t:P * (t + 1)],
                                        o_T[:, half, P * t:P * (t + 1)], ident[:, :])
                last.then_inc(a_full, 1)

            def turn_all(slot, u):
                b = u // 2
                for t in range(4):
                    last = pe.transpose(banks[:, A_BANK + slot, P * t:P * (t + 1)],
                                        attn[:, 4 * (u % 2) + t, GB * b:GB * (b + 1), :].rearrange("p g w -> p (g w)"),
                                        ident[:, :])
                last.then_inc(a_full, 1)

            def project(slot, u):
                for t in range(4):
                    last = pe.matmul(banks[:, A_BANK + slot, P * t:P * (t + 1)], attnT[:, u, P * t:P * (t + 1)],
                                     wo_sb[:, :], start=True, stop=True)
                last.then_inc(a_full, 1)

            def turn(i, r):
                first, units = ring_base(i, r), turn_units(i, r)

                def pass_ring(t, place, head=None):
                    for u, (at, where, kind, h) in enumerate(units):
                        if (at, where) != (t, place) or (place == "beside" and h != head):
                            continue
                        slot = (ring_const(i, r) + u) % A_RING
                        pe.wait_ge(a_free, first + u - A_RING + 1)
                        if kind == "rows":
                            rows(slot, i, r + 1, t, h)
                        elif kind == "max1":
                            maxima_up(slot, i, r, 1)
                        elif kind == "max0":
                            maxima_up(slot, i, r + 1, 0)
                        elif kind == "out1":
                            outputs_up(slot, i, r - 1, 1)
                        elif kind == "out0":
                            outputs_up(slot, i, r, 0)
                        elif kind == "turn":
                            if h == 2:
                                pe.wait_ge(a_free, ring_at(0, GROUPS - 1, "out0") + 1)
                            turn_all(slot, h)
                        else:
                            pe.wait_ge(a_free, ring_at(0, GROUPS - 1, "turn", h) + 1)
                            project(slot, h)

                for t in range(STEPS):
                    pass_ring(t, "before")
                    for what in ORDER[len(heads_of(t))]:
                        if what[0] == "B":
                            cols(i, r, t, int(what[1]))
                        else:
                            pass_ring(t, "beside", int(what[1]))
                    pass_ring(t, "after")
                    if t >= 2:
                        products(i, r, t - 2)
                    elif not is_first(i, r):
                        products(i, r - 1, t + STEPS - 2)

            pe.wait_ge(pool_const, 5)
            pe.wait_ge(wqk_in, 32)
            pe.wait_ge(wo_in, 16)
            start_unit(("scale",))
            for unit in WAY_IN + BEFORE_A:
                start_unit(unit)
            pe.wait_ge(rows_in, 2 * SLOTS * 16)
            pe.wait_ge(pool_const, 11)
            for who in ("act", "dve"):
                pe.wait_ge(start_emptied[0][who], all_emptied(0, who))
            for t in range(STEPS):
                if t == 5:
                    pe.wait_ge(a_free, GH * 5 - A_RING + 1)
                    maxima_up(GH * 5 % A_RING, 0, 0, 0)
                for h in range(GH):
                    u = GH * t + h + (t >= 5)
                    if u >= A_RING:
                        pe.wait_ge(a_free, u - A_RING + 1)
                    rows(u % A_RING, 0, 0, t, h)
                for unit in AFTER_STEP[t]:
                    start_unit(unit)
            for who in ("act", "dve"):
                pe.wait_ge(start_emptied[1][who], all_emptied(1, who))

            turn(0, 0)
            with pe.Fori(0, (GROUPS - 2) // 3) as i:
                for r in (1, 2, 3):
                    turn(i, r)
            turn(0, GROUPS - 1)
            products(0, GROUPS - 1, STEPS - 2)
            products(0, GROUPS - 1, STEPS - 1)
            pe.wait_ge(a_free, END - A_RING + 1)
            outputs_up(END % A_RING, 0, GROUPS - 1, 1)
            pe.wait_ge(a_free, END + 1)
            turn_all((END + 1) % A_RING, 3)
            pe.wait_ge(a_free, END + 2)
            project((END + 2) % A_RING, 3)
    return nc


def kernel(L0_attn_x, L0_attn_w_qkv, L0_attn_w_out, L0_ffn_W1, L0_ffn_b1, L0_ffn_W2, L0_ffn_b2):
    import numpy as np
    import concourse.bacc as bacc
    from concourse.bass_utils import run_bass_kernel_spmd

    wqkv = np.ascontiguousarray(np.asarray(L0_attn_w_qkv).T)
    wswap = np.ascontiguousarray(wqkv[:, :2 * D].reshape(D, 2 * HEADS, 2, HD // 2)[:, :, ::-1, :].reshape(D, 2 * D))
    wo = np.ascontiguousarray(np.asarray(L0_attn_w_out).T)
    w1 = np.ascontiguousarray(np.asarray(L0_ffn_W1).T)
    w2 = np.ascontiguousarray(np.asarray(L0_ffn_W2).T.reshape(FF // P, P, D).transpose(1, 0, 2))
    b1 = np.ascontiguousarray(np.asarray(L0_ffn_b1).reshape(FF // P, P).T)
    b2 = np.ascontiguousarray(np.asarray(L0_ffn_b2).reshape(1, D))

    half = HD // 2
    inv_freq = (1.0 / np.float32(10000.0) ** (np.arange(half, dtype=np.float32) / half)).astype(np.float32)
    freqs = np.arange(SEQ, dtype=np.float32)[None, :] * inv_freq[:, None]
    cos = np.tile(np.cos(freqs).astype(np.float32), (2 * HEADS, 1))
    sin = np.tile(np.concatenate([-np.sin(freqs), np.sin(freqs)]).astype(np.float32), (HEADS, 1))

    const_rows = np.zeros((B_ROWS - PAIRS, 2 * GH * BANK), mybir.dt.np(BF16))
    const_rows[A_ROWS - PAIRS:] = -1

    arrays = {"x": np.ascontiguousarray(L0_attn_x), "wqkv": wqkv, "wswap": wswap, "wo": wo, "w1": w1, "b1": b1,
              "w2": w2, "b2": b2, "cos": cos, "sin": sin, "const_rows": const_rows}
    nc = bacc.Bacc("TRN2", target_bir_lowering=False, num_devices=1)
    args = {name: nc.dram_tensor(name, a.shape, mybir.dt.from_np(a.dtype), kind="ExternalInput").ap()
            for name, a in arrays.items()}
    out = nc.dram_tensor("out", (BATCH, SEQ, D), F32, kind="ExternalOutput").ap()
    build(nc, out=out, **args)
    return run_bass_kernel_spmd(nc, [arrays], core_ids=[0]).results[0]["out"]
```
